# Optimizing a Trainium2 kernel written in Bass

```python
import numpy as np
import jax
import jax.numpy as jnp

def _softmax(x, axis=-1):
    return jax.nn.softmax(x, axis=axis)
def _gelu(x):
    return jax.nn.gelu(x, approximate=True)
def _silu(x):
    return jax.nn.silu(x)
def _sigmoid(x):
    return jax.nn.sigmoid(x)
def _layernorm(x, axis=-1, eps=1e-5):
    m = jnp.mean(x, axis=axis, keepdims=True)
    v = jnp.var(x, axis=axis, keepdims=True)
    return (x - m) / jnp.sqrt(v + eps)
def _scatter_add(tgt, idx, src, axis=0):
    return tgt.at[idx].add(src)
def _segment_sum(src, seg, n):
    return jax.ops.segment_sum(src, seg, n)

kernel_name = 'mk_conv_preact_d1_conv_nchw256_05f956'

def setup_inputs(seed: int = 0):
    np.random.seed(seed)
    _w = jnp.asarray
    def _rec_inputs():
        import jax
        import jax.numpy as jnp
        _gk = jax.random.key(seed)
        x = -8.268e-05 + 0.9999 * jax.random.normal(jax.random.fold_in(_gk, 1), (64, 256, 56, 56), jnp.float32)
        return x
    x = _rec_inputs()
    def _L0_conv_setup():
        import jax, jax.numpy as jnp
        import numpy as np
        SPATIAL = 56
        PLANES = 256
        REDUCTION = 16
        REMOVED_RATIO = 0.5
        SPATIAL_IN = SPATIAL * SPATIAL
        HIDDEN = SPATIAL_IN // REDUCTION
        REMOVED_NUM = int(np.round(SPATIAL_IN * REMOVED_RATIO))
        key = jax.random.key(seed)
        k1, k2, k3 = jax.random.split(key, 3)
        B = 64
        x = jax.random.normal(k1, (B, PLANES, SPATIAL, SPATIAL), dtype=jnp.float32)
        W1 = jax.random.normal(k2, (HIDDEN, SPATIAL_IN), dtype=jnp.float32) / np.sqrt(SPATIAL_IN)
        W2 = jax.random.normal(k3, (SPATIAL_IN, HIDDEN), dtype=jnp.float32) / np.sqrt(HIDDEN)
        return {'x': x, 'W1': W1, 'W2': W2}
    _L0_conv_all = _L0_conv_setup()
    _L0_conv_in = {k: v for k, v in _L0_conv_all.items() if k in ('W1', 'W2', )}
    del _L0_conv_all

    return {
        "x": x,
        "L0_conv_W1": _L0_conv_in["W1"],
        "L0_conv_W2": _L0_conv_in["W2"],
    }

def reference(x, L0_conv_W1, L0_conv_W2):
    import jax
    import jax.numpy as jnp
    def _L0_conv_ref(x, W1, W2):
        import jax, jax.numpy as jnp
        import numpy as np
        SPATIAL = 56
        PLANES = 256
        REDUCTION = 16
        REMOVED_RATIO = 0.5
        SPATIAL_IN = SPATIAL * SPATIAL
        HIDDEN = SPATIAL_IN // REDUCTION
        REMOVED_NUM = int(np.round(SPATIAL_IN * REMOVED_RATIO))
        b, c, h, w = x.shape
        y = jnp.mean(x, axis=1).reshape(b, h * w)
        y = jax.nn.relu(jnp.einsum('bi,oi->bo', y, W1))
        y = jax.nn.sigmoid(jnp.einsum('bh,oh->bo', y, W2))
        idx = jnp.argsort(jnp.abs(y), axis=1)[:, :REMOVED_NUM]
        rows = jnp.arange(b)[:, None]
        y = y.at[rows, idx].set(0.0)
        y = y.reshape(b, 1, SPATIAL, SPATIAL)
        return jnp.broadcast_to(y, (b, PLANES, SPATIAL, SPATIAL))

    def _gn(v, G=32, eps=1e-5):
        B_, C_, H_, W_ = v.shape
        g = v.reshape(B_, G, C_ // G, H_, W_)
        m = jnp.mean(g, axis=(2, 3, 4), keepdims=True)
        s = jnp.var(g, axis=(2, 3, 4), keepdims=True)
        return ((g - m) / jnp.sqrt(s + eps)).reshape(v.shape)

    def _ln_c(v, eps=1e-6):
        m = jnp.mean(v, axis=1, keepdims=True)
        s = jnp.var(v, axis=1, keepdims=True)
        return (v - m) / jnp.sqrt(s + eps)

    def _ln_t(v, eps=1e-5):
        m = jnp.mean(v, axis=-1, keepdims=True)
        s = jnp.var(v, axis=-1, keepdims=True)
        return (v - m) / jnp.sqrt(s + eps)

    def _to_tokens(v):
        B_, C_, H_, W_ = v.shape
        return v.reshape(B_, C_, H_ * W_).transpose(0, 2, 1)
    def _from_tokens(t, like):
        B_, C_, H_, W_ = like.shape
        return t.transpose(0, 2, 1).reshape(B_, C_, H_, W_)

    x = x + _L0_conv_ref(_gn(x), L0_conv_W1, L0_conv_W2)
    return x


_drawn_inputs = setup_inputs


def setup_inputs(seed=0):
    import zlib

    import numpy as np

    out = dict(_drawn_inputs(seed))
    spreads = {}
    factors = {}
    for name, (base, spread) in spreads.items():
        noise = np.random.default_rng([zlib.crc32(name.encode()), seed]).standard_normal(out[name].shape)
        drawn = base * np.exp(spread * noise) if base else spread * noise
        out[name] = jnp.asarray(drawn.astype(out[name].dtype))
    for name, factor in factors.items():
        out[name] = (out[name] * factor).astype(out[name].dtype)
    return out
```

```python
from contextlib import ExitStack

import numpy as np

import concourse.bass as bass
from concourse import mybir

F32, I32, BF16, I16 = mybir.dt.float32, mybir.dt.int32, mybir.dt.bfloat16, mybir.dt.int16
ALU, ACT, AX = mybir.AluOpType, mybir.ActivationFunctionType, mybir.AxisListType

P = 128
CHANNELS, PIXELS, GROUPS, HIDDEN = 256, 56 * 56, 32, 196
CUT = PIXELS // 2
EPS = 1e-5
PAIR_SLOTS = 3
QUARTERS, COPIES = 4, 16
QUARTER = PIXELS // QUARTERS
BANK = QUARTER // 2
CHUNK = 112
CHUNKS = QUARTER // CHUNK
HALF_HIDDEN = HIDDEN // 2
PER_GROUP = (CHANNELS // GROUPS) * PIXELS
BITS, STEPS = 4, 8
PARTS = 7
ADDS = 2 * QUARTERS


def constants():
    p = np.arange(P)
    quarter, copy, image = p // 32, p % 32 // 2, p % 2
    channel_to_rows = (p[:, None] // 4 == p % 32).astype(np.float32)
    row_to_rows = (p[:, None] % 32 == p % 32).astype(np.float32)
    row_to_channels = (p[:, None] % 32 == p // 4).astype(np.float32)
    own = (image[:, None] == np.arange(32) % 2).astype(np.float32)
    before = ((image[:, None] == image) & (quarter[:, None] < quarter) & (copy[:, None] == 0)).astype(np.float32)
    block = (quarter[:, None] == np.arange(QUARTERS)).astype(np.float32) / CHANNELS
    first = (p[:, None] == 32 * (np.arange(8) // 2) + np.arange(8) % 2).astype(np.float32)
    exponent = np.full((P, 1), -0.5, np.float32)
    zero = np.zeros((P, 1), np.float32)
    number = np.arange(32) // 2
    shifts = [BITS * (STEPS - 1 - k) for k in range(STEPS)]
    top = 4
    weights = np.zeros((P, STEPS, 32), np.float32)
    bits = np.zeros((P, STEPS + 1), np.int32)
    for k, shift in enumerate(shifts):
        valid = (number > 0) & ((number < top) | (k > 0))
        weights[:, k] = own * np.where(valid, (number ^ (number - 1)) << shift, 0)
        bits[:, k] = np.where((copy < top) | (k > 0), copy, 0).astype(np.int64) << shift
    turns = np.concatenate([bits[:, :1], bits[:, :-1] ^ bits[:, 1:]], 1).astype(np.int32)
    parts = [channel_to_rows, row_to_rows, row_to_channels, own, before, block, first, exponent, zero]
    table = np.concatenate([*parts, weights.reshape(P, -1)], 1)
    return np.ascontiguousarray(table), turns


def gate_kernel(nc, x, w1, w2, table, turns, out):
    images = x.shape[0]
    pairs = images // 2
    rounds, rest = divmod(pairs, PAIR_SLOTS)
    x_v = x.rearrange("n (p t) h w -> n p t (h w)", p=P)
    out_v = out.rearrange("n (p t) h w -> n p t (h w)", p=P)

    with ExitStack() as ctx:
        def sb(name, shape, dtype=F32):
            return ctx.enter_context(nc.sbuf_tensor(name, shape, dtype))

        def ps(name, shape):
            return ctx.enter_context(nc.psum_tensor(name, shape, F32))

        def sem(name):
            return ctx.enter_context(nc.semaphore(name))

        xs = sb("xs", [P, 2 * PAIR_SLOTS, 2, PIXELS])
        w1_sb = sb("w1_sb", [CHUNK, CHUNKS * QUARTERS, HIDDEN])
        w2_sb = sb("w2_sb", [HALF_HIDDEN, 2, PIXELS])
        consts = sb("consts", [P, table.shape[1]])
        turn = sb("turn", [P, STEPS + 1], I32)
        group_sums = sb("group_sums", [P, QUARTER])
        small = sb("small", [P, 28])
        row_sums = small[:, 0:2]
        minus_mean = small[:, 2:4]
        variance, inv_std, below = (small[:, c:c + 1] for c in range(4, 7))
        candidate = small[:, 7:8].bitcast(I32)
        squares = small[:, 8:8 + PARTS]
        coef = small[:, 15:15 + QUARTERS]
        rank = small[:, 19:21]
        unread = small[:, 21:21 + PARTS]
        pixels = sb("pixels", [CHUNK, CHUNKS * QUARTERS, 2])
        hidden = sb("hidden", [HALF_HIDDEN, 2, 32])
        gate = sb("gate", [P, QUARTER])
        masked = sb("masked", [P, QUARTER])
        ties = sb("ties", [P, QUARTER], BF16)
        kept = sb("kept", [P, 33], I32)
        own_totals = sb("own_totals", [P, 32])

        at = 0

        def part(n):
            nonlocal at
            at += n
            return consts[:, at - n:at]

        channel_to_rows, row_to_rows, row_to_channels = part(P), part(P), part(P)
        own, before = part(32), part(P)
        block_mask, first_copy, exponent, zero = part(QUARTERS), part(8), part(1), part(1)
        weights = part(STEPS * 32)

        sums_ps = ps("sums_ps", [P, 2, 512])
        net_ps = ps("net_ps", [P, 2, 512])
        stat_ps = ps("stat_ps", [P, 512])
        count_ps = ps("count_ps", [P, 512])
        spread_ps = ps("spread_ps", [P, 2, 512])
        mean_ps, mean8_ps, var_ps = stat_ps[:, 0:1], stat_ps[:, 1:2], stat_ps[:, 2:2 + PARTS]
        pixel_ps = stat_ps[0:CHUNK, 16:16 + CHUNKS * QUARTERS]
        part_size = 2 * PIXELS // PARTS
        unread_squares = sums_ps[:].rearrange("p b n -> p (b n)")[:, 0:part_size]
        parts_ps = net_ps[:, 0, 0:HIDDEN]
        hidden_ps = net_ps[0:HALF_HIDDEN, 1, 0:64]
        totals_ps, before_ps = count_ps[:, 0:32], count_ps[:, 32:33]

        const_in = sem("const_in")
        parts_sb = group_sums[:, 0:HIDDEN]

        w1_in = sem("w1_in")
        w2_in = sem("w2_in")
        loaded = [[sem(f"loaded_{i}_{h}") for h in range(2)] for i in range(2 * PAIR_SLOTS)]
        stored = [sem(f"stored_{i}") for i in range(2 * PAIR_SLOTS)]
        sums_made = sem("sums_made")
        sums_kept = sem("sums_kept")
        means_made = sem("means_made")
        means_kept = sem("means_kept")
        squared = sem("squared")
        var_made = sem("var_made")
        var_kept = sem("var_kept")
        inv_made = sem("inv_made")
        coef_made = sem("coef_made")
        pixels_made = sem("pixels_made")
        pixels_kept = sem("pixels_kept")
        parts_made = sem("parts_made")
        parts_kept = sem("parts_kept")
        hidden_made = sem("hidden_made")
        hidden_kept = sem("hidden_kept")
        logits_made = sem("logits_made")
        gate_made = sem("gate_made")
        counted = sem("counted")
        totalled = sem("totalled")
        dve_step = sem("dve_step")
        masked_made = sem("masked_made")
        spread_made = sem("spread_made")
        added = sem("added")

        block = ctx.enter_context(nc.Block())

        def each_pair(eng, body):
            if rounds:
                with eng.Fori(0, rounds) as r:
                    for s in range(PAIR_SLOTS):
                        body(s, lambda per, add=0, r=r, s=s: r * (PAIR_SLOTS * per) + (s * per + add), r)
            for s in range(rest):
                body(s, lambda per, add=0, s=s: (rounds * PAIR_SLOTS + s) * per + add, rounds)

        @block.sync
        def _(sp):
            sp.dma_start(consts[:], table).then_inc(const_in, 16)
            sp.dma_start(turn[:], turns).then_inc(const_in, 16)

            def load(slot, n):
                for h in range(2):
                    cols = slice(h * CUT, (h + 1) * CUT)
                    sp.dma_start(xs[:, slot, :, cols], x_v[n, :, :, cols]).then_inc(loaded[slot][h], 16)

            for n in range(2 * PAIR_SLOTS):
                load(n, n)
                if n == 1:
                    sp.dma_start(w1_sb[:], w1).then_inc(w1_in, 16)
                    sp.dma_start(w2_sb[:], w2).then_inc(w2_in, 16)

            def image(slot, n, r, reload, r_before):
                for h in range(2):
                    cols = slice(h * CUT, (h + 1) * CUT)
                    sp.wait_ge(added, n * ADDS + (h + 1) * (ADDS // 2))
                    sp.dma_start(out_v[n, :, :, cols], xs[:, slot, :, cols]).then_inc(stored[slot], 16)
                    if h == 0 and reload:
                        last = (slot - 1) % (2 * PAIR_SLOTS)
                        sp.wait_ge(stored[last], (r_before + 1) * 32)
                        load(last, n - 1 + 2 * PAIR_SLOTS)

            slots = 2 * PAIR_SLOTS
            looped = max(0, (images + 1) // slots - 2)
            for n in range(slots):
                image(n, n, 0, n > 0 and n - 1 + slots < images, 0)
            if looped > 0:
                with sp.Fori(1, looped + 1) as r:
                    for slot in range(slots):
                        image(slot, r * slots + slot, r, True, r - (slot == 0))
            for n in range((looped + 1) * slots, images):
                image(n % slots, n, n // slots, n - 1 + slots < images, (n - 1) // slots)
            for slot in range(slots):
                sp.wait_ge(stored[slot], 32 * len(range(slot, images, slots)))

        @block.tensor
        def _(pe):
            t = nc.tensor

            def wide(column, m, k=P):
                return column.to_broadcast([k, m])

            def sums(slot, b, t2, n, r):
                if t2 == 0:
                    pe.wait_ge(loaded[slot][b], (r + 1) * 16)
                    if b == 0:
                        pe.wait_ge(squared, n * PARTS)
                for q in range(QUARTERS):
                    lo = b * CUT + q * BANK
                    last = t.matmul(sums_ps[32 * q:32 * q + 32, b, 0:BANK], channel_to_rows[:, 0:32],
                                    xs[:, slot, t2, lo:lo + BANK], start=t2 == 0, stop=t2 == 1)
                if b == 1 and t2 == 1:
                    last.then_inc(sums_made, 1)

            def means(n):
                pe.wait_ge(sums_kept, n + 1)
                pe.wait_ge(pixels_kept, n)
                for b in range(2):
                    t.matmul(mean_ps, row_to_channels, row_sums[:, b:b + 1], start=b == 0, stop=b == 1)
                for b in range(2):
                    last = t.matmul(mean8_ps, row_to_rows, row_sums[:, b:b + 1], start=b == 0, stop=b == 1)
                last.then_inc(means_made, 1)

            def var(n):
                pe.wait_ge(squared, n * PARTS + PARTS)
                t.matmul(var_ps, channel_to_rows, squares, start=True, stop=True).then_inc(var_made, 1)

            def to_pixels(n):
                pe.wait_ge(coef_made, n + 1)
                t.matmul(pixel_ps, wide(minus_mean[:, 1:2], CHUNK),
                         coef.unsqueeze(1).to_broadcast([P, CHUNKS, QUARTERS]), start=True, stop=False)
                for k in range(CHUNKS):
                    last = t.matmul(pixel_ps[:, k * QUARTERS:(k + 1) * QUARTERS],
                                    group_sums[:, k * CHUNK:(k + 1) * CHUNK], coef,
                                    start=False, stop=k == CHUNKS - 1)
                last.then_inc(pixels_made, 1)

            def layers(i):
                pe.wait_ge(pixels_kept, i(2, 2))
                pe.wait_ge(gate_made, i(1))
                for q in range(QUARTERS):
                    t.matmul(parts_ps[32 * q:32 * q + 32, :], wide(zero[0:CHUNK], 32, CHUNK),
                             w1_sb[:, q, :], start=True, stop=False)
                for k in range(CHUNKS):
                    for q in range(QUARTERS):
                        c = k * QUARTERS + q
                        last = t.matmul(parts_ps[32 * q:32 * q + 2, :], pixels[:, c, :],
                                        w1_sb[:, c, :], start=False, stop=k == CHUNKS - 1)
                last.then_inc(parts_made, 1)
                pe.wait_ge(parts_kept, i(1, 1))
                for u in range(2):
                    last = t.matmul(hidden_ps[:, 32 * u:32 * u + 32],
                                    parts_sb[:, u * HALF_HIDDEN:(u + 1) * HALF_HIDDEN],
                                    row_to_rows[:, 0:2].unsqueeze(1).to_broadcast([P, COPIES, 2]),
                                    start=True, stop=True)
                last.then_inc(hidden_made, 1)
                pe.wait_ge(hidden_kept, i(1, 1))
                for b in range(2):
                    for u in range(2):
                        for q in range(QUARTERS):
                            lo = q * QUARTER + b * BANK
                            last = t.matmul(net_ps[32 * q:32 * q + 32, b, 0:BANK], hidden[:, u, :],
                                            w2_sb[:, u, lo:lo + BANK], start=u == 0, stop=u == 1)
                last.then_inc(logits_made, 1)

            def totals(i, k):
                pe.wait_ge(counted, i(STEPS + 1, k + 1))
                t.matmul(totals_ps, wide(below, P), row_to_rows[:, 0:32], start=True, stop=True).then_inc(totalled, 1)

            def ties_before(i):
                pe.wait_ge(counted, i(STEPS + 1, STEPS + 1))
                t.matmul(before_ps, before, below, start=True, stop=True).then_inc(totalled, 1)

            def spread(i, a, c):
                if a == 0 and c == 0:
                    pe.wait_ge(masked_made, i(1, 2))
                n = a * ADDS + c
                if n >= 2:
                    pe.wait_ge(added, i(2 * ADDS, n - 1))
                q, b = divmod(c, 2)
                t.matmul(spread_ps[:, c % 2, 0:BANK], wide(first_copy[:, 2 * q + a:2 * q + a + 1], P),
                         masked[:, b * BANK:(b + 1) * BANK], start=True, stop=True).then_inc(spread_made, 1)

            def stats(s, a, n, r):
                slot = 2 * s + a
                for b in range(2):
                    for t2 in range(2):
                        sums(slot, b, t2, n, r)
                means(n)
                var(n)
                to_pixels(n)

            def body(s, i, r, following=None):
                if following is None:
                    for k in range(STEPS):
                        totals(i, k)
                    ties_before(i)
                    for a in range(2):
                        for c in range(ADDS):
                            spread(i, a, c)
                    return
                s1, i1, r1 = following
                for k in range(STEPS):
                    totals(i, k)
                    if k < 4:
                        sums(2 * s1, k // 2, k % 2, i1(2), r1)
                    if k == 4:
                        means(i1(2))
                ties_before(i)
                var(i1(2))
                to_pixels(i1(2))
                for b in range(2):
                    for t2 in range(2):
                        sums(2 * s1 + 1, b, t2, i1(2, 1), r1)
                for a in range(2):
                    for c in range(ADDS):
                        spread(i, a, c)
                        if (a, c) == (0, 3):
                            means(i1(2, 1))
                        if (a, c) == (1, 3):
                            var(i1(2, 1))
                        if (a, c) == (1, 5):
                            to_pixels(i1(2, 1))
                layers(i1)

            pe.wait_ge(const_in, 32)
            at0 = lambda per, add=0: add
            stats(0, 0, 0, 0)
            stats(0, 1, 1, 0)
            pe.wait_ge(w1_in, 16)
            pe.wait_ge(w2_in, 16)
            layers(at0)

            def after(s, r):
                carry, s1 = divmod(s + 1, PAIR_SLOTS)
                r1 = r + carry
                return s1, lambda per, add=0: r1 * (PAIR_SLOTS * per) + (s1 * per + add), r1

            full = (pairs - 1) // PAIR_SLOTS
            if full:
                with pe.Fori(0, full) as r:
                    for s in range(PAIR_SLOTS):
                        body(s, lambda per, add=0, s=s: r * (PAIR_SLOTS * per) + (s * per + add), r, after(s, r))
            for pair in range(full * PAIR_SLOTS, pairs):
                s, r = pair % PAIR_SLOTS, pair // PAIR_SLOTS
                i = lambda per, add=0, pair=pair: pair * per + add
                body(s, i, r, after(s, r) if pair + 1 < pairs else None)

        @block.scalar
        def _(act):
            sc = nc.scalar
            act.wait_ge(const_in, 32)

            def body(s, i, r):
                for a in range(2):
                    slot, n = 2 * s + a, i(2, a)
                    act.wait_ge(sums_made, n + 1)
                    if a == 1:
                        act.wait_ge(pixels_made, n)
                    for b in range(2):
                        last = sc.activation(group_sums[:, b * BANK:(b + 1) * BANK], sums_ps[:, b, 0:BANK],
                                             ACT.Copy, accum_out=row_sums[:, b:b + 1])
                    last.then_inc(sums_kept, 1)
                    act.wait_ge(means_made, n + 1)
                    sc.mul(minus_mean[:, 0:1], mean_ps, -1.0 / PER_GROUP)
                    sc.mul(minus_mean[:, 1:2], mean8_ps, -8.0 / PER_GROUP).then_inc(means_kept, 1)
                    act.wait_ge(means_kept, n + 1)
                    flat = xs[:, slot].rearrange("p t n -> p (t n)")
                    for j in range(PARTS):
                        if j:
                            act.wait_ge(squared, n * PARTS + j)
                        sc.activation(unread_squares, flat[:, j * part_size:(j + 1) * part_size], ACT.Square,
                                      bias=minus_mean[:, 0:1], accum_out=squares[:, j:j + 1]).then_inc(squared, 1)
                    act.wait_ge(var_made, n + 1)
                    sc.activation(unread, var_ps, ACT.Copy, bias=EPS / PARTS, scale=1.0 / PER_GROUP,
                                  accum_out=variance).then_inc(var_kept, 1)
                    act.wait_ge(pixels_made, n + 1)
                    sc.copy(pixels[:, :, a], pixel_ps).then_inc(pixels_kept, 1)
                act.wait_ge(parts_made, i(1, 1))
                sc.copy(parts_sb, parts_ps).then_inc(parts_kept, 1)
                act.wait_ge(hidden_made, i(1, 1))
                sc.activation(hidden[:].rearrange("p u m -> p (u m)"), hidden_ps, ACT.Relu).then_inc(hidden_kept, 1)
                act.wait_ge(logits_made, i(1, 1))
                act.wait_ge(masked_made, i(1, 1))
                sc.activation(gate[:].rearrange("p (b n) -> p b n", b=2), net_ps[:, :, 0:BANK],
                              ACT.Sigmoid).then_inc(gate_made, 1)

            each_pair(act, body)

        @block.gpsimd
        def _(pool):
            pool.wait_ge(const_in, 32)

            def body(s, i, r):
                for a in range(2):
                    n = i(2, a)
                    pool.wait_ge(var_kept, n + 1)
                    nc.gpsimd.tensor_tensor(inv_std, variance, exponent, ALU.pow).then_inc(inv_made, 1)
                    pool.wait_ge(inv_made, n + 1)
                    if a == 1:
                        pool.wait_ge(pixels_made, n)
                    nc.gpsimd.tensor_tensor(coef, block_mask, inv_std.to_broadcast([P, QUARTERS]), ALU.mult).then_inc(coef_made, 1)

            each_pair(pool, body)

        @block.vector
        def _(dve):
            v = nc.vector
            dve.wait_ge(const_in, 32)
            dve.sem_inc(masked_made, 1)
            CHAIN = 2 * STEPS + 7

            def body(s, i, r):
                done = [0]

                def step(instruction):
                    done[0] += 1
                    instruction.then_inc(dve_step, 1)
                    dve.wait_ge(dve_step, i(CHAIN, done[0]))

                step(v.tensor_copy(candidate, turn[:, 0:1]))
                dve.wait_ge(gate_made, i(1, 1))
                value = small[:, 7:8]
                for k in range(STEPS):
                    v.tensor_scalar(ties[:], gate[:], value, None, ALU.is_lt, ALU.add,
                                    accum_out=below).then_inc(counted, 1)
                    v.tensor_tensor(kept[:, 32:33], candidate, turn[:, k + 1:k + 2] if k + 1 < STEPS else
                                    turn[:, STEPS:STEPS + 1], ALU.bitwise_xor)
                    dve.wait_ge(totalled, i(STEPS + 1, k + 1))
                    if k == STEPS - 1:
                        v.tensor_tensor(own_totals[:], totals_ps, own, ALU.mult)
                    step(v.scalar_tensor_tensor(kept[:, 0:32], totals_ps, CUT - 0.5, weights[:, 32 * k:32 * k + 32],
                                                ALU.is_lt, ALU.mult))
                    step(v.tensor_reduce(candidate, kept[:], AX.X, ALU.bitwise_xor))
                v.tensor_scalar(ties[:], gate[:], value, None, ALU.is_equal, ALU.add,
                                accum_out=below).then_inc(counted, 1)
                step(v.scalar_tensor_tensor(own_totals[:], own_totals[:], CUT - 0.5, own_totals[:],
                                            ALU.is_lt, ALU.mult))
                step(v.tensor_reduce(rank[:, 0:1], own_totals[:], AX.X, ALU.max))
                dve.wait_ge(totalled, i(STEPS + 1, STEPS + 1))
                step(v.tensor_tensor(rank[:, 1:2], rank[:, 0:1], before_ps, ALU.add))
                position = masked[:].bitcast(I16)[:, 0:QUARTER]
                step(v.tensor_tensor_scan(position, ties[:], ties[:], rank[:, 1:2], ALU.add, ALU.max))
                step(v.scalar_tensor_tensor(ties[:], position, CUT + 0.5, ties[:], ALU.is_gt, ALU.mult))
                step(v.scalar_tensor_tensor(ties[:], gate[:], value, ties[:], ALU.is_gt, ALU.max))
                v.tensor_tensor(masked[:], gate[:], ties[:], ALU.mult).then_inc(masked_made, 1)
                assert done[0] == CHAIN, done
                for a in range(2):
                    for c in range(ADDS):
                        dve.wait_ge(spread_made, i(2 * ADDS, a * ADDS + c + 1))
                        piece = xs[:, 2 * s + a, :, c * BANK:(c + 1) * BANK]
                        v.tensor_tensor(piece, piece,
                                        spread_ps[:, c % 2, 0:BANK].unsqueeze(1).to_broadcast([P, 2, BANK]),
                                        ALU.add).then_inc(added, 1)

            each_pair(dve, body)


def kernel(x, L0_conv_W1, L0_conv_W2):
    import concourse.bacc as bacc
    from concourse.bass_utils import run_bass_kernel_spmd

    w1 = np.asarray(L0_conv_W1).reshape(HIDDEN, 2, QUARTERS, BANK).transpose(0, 2, 1, 3)
    w1 = w1.reshape(HIDDEN, QUARTERS, CHUNKS, CHUNK).transpose(3, 2, 1, 0)
    w1 = np.ascontiguousarray(w1.reshape(CHUNK, CHUNKS * QUARTERS, HIDDEN))
    w2 = np.asarray(L0_conv_W2).T.reshape(2, HALF_HIDDEN, PIXELS).transpose(1, 0, 2)
    table, turns = constants()
    arrays = {"x": np.ascontiguousarray(x), "w1": w1, "w2": np.ascontiguousarray(w2), "table": table, "turns": turns}

    nc = bacc.Bacc("TRN2", target_bir_lowering=False, num_devices=1)
    ins = [nc.dram_tensor(k, a.shape, mybir.dt.from_np(a.dtype), kind="ExternalInput").ap() for k, a in arrays.items()]
    out = nc.dram_tensor("out", arrays["x"].shape, F32, kind="ExternalOutput").ap()
    gate_kernel(nc, *ins, out)
    result = run_bass_kernel_spmd(nc, [arrays], core_ids=[0])
    return result.results[0]["out"]
```

```python
from contextlib import ExitStack

import numpy as np

import concourse.bass as bass
from concourse import mybir

F32, F16, BF16 = mybir.dt.float32, mybir.dt.float16, mybir.dt.bfloat16
I32, I16, U16, U8 = mybir.dt.int32, mybir.dt.int16, mybir.dt.uint16, mybir.dt.uint8
ALU, ACT, AX = mybir.AluOpType, mybir.ActivationFunctionType, mybir.AxisListType

P = 128
CHANNELS, PIXELS, GROUPS, HIDDEN = 256, 56 * 56, 32, 196
CUT = PIXELS // 2
EPS = 1e-5
PAIR_SLOTS = 3
QUARTERS, COPIES = 4, 16
QUARTER = PIXELS // QUARTERS
BANK = QUARTER // 2
CHUNK = 112
CHUNKS = QUARTER // CHUNK
HALF_HIDDEN = HIDDEN // 2
PER_GROUP = (CHANNELS // GROUPS) * PIXELS
BITS, STEPS = 4, 8
PARTS = 8
ADDS = 2 * QUARTERS


def constants():
    p = np.arange(P)
    quarter, copy, image = p // 32, p % 32 // 2, p % 2
    channel_to_rows = (p[:, None] // 4 == p % 32).astype(np.float32)
    row_to_rows = (p[:, None] % 32 == p % 32).astype(np.float32)
    row_to_channels = (p[:, None] % 32 == p // 4).astype(np.float32)
    own = (image[:, None] == np.arange(32) % 2).astype(np.float32)
    before = ((image[:, None] == image) & (quarter[:, None] < quarter) & (copy[:, None] == 0)).astype(np.float32)
    block = (quarter[:, None] == np.arange(QUARTERS)).astype(np.float32) / CHANNELS
    terms = (p[:, None] // 32 == np.arange(8) // 2) & (p[:, None] % 2 == np.arange(8) % 2) & (p[:, None] % 32 < 6)
    less = -np.stack([copy >= 1, copy >= 2], 1).astype(np.float32)
    exponent = np.full((P, 1), -0.5, np.float32)
    number = np.arange(32) // 2
    shifts = [BITS * (STEPS - 1 - k) for k in range(STEPS)]
    top = 4
    weights = np.zeros((P, STEPS, 32), np.float32)
    bits = np.zeros((P, STEPS + 1), np.int32)
    for k, shift in enumerate(shifts):
        valid = (number > 0) & ((number < top) | (k > 0))
        weights[:, k] = own * np.where(valid, (number ^ (number - 1)) << shift, 0)
        bits[:, k] = np.where((copy < top) | (k > 0), copy, 0).astype(np.int64) << shift
    turns = np.concatenate([bits[:, :1], bits[:, :-1] ^ bits[:, 1:]], 1).astype(np.int32)
    table = np.concatenate([channel_to_rows, row_to_rows, row_to_channels, block, less, exponent], 1)
    halves = np.concatenate([before, row_to_rows[:, 0:32], own], 1).astype(np.float16).view(np.uint16)
    wide_range = np.concatenate([terms.astype(np.float32), weights.reshape(P, -1)], 1)
    wide_range = (wide_range.view(np.uint32) >> 16).astype(np.uint16)
    return table, np.concatenate([halves, wide_range, turns.view(np.uint16)], 1)


def gate_kernel(nc, x, w1, w2, table, count_table, out):
    images = x.shape[0]
    pairs = images // 2
    x_v = x.rearrange("n (p t) h w -> n p t (h w)", p=P)
    out_v = out.rearrange("n (p t) h w -> n p t (h w)", p=P)

    with ExitStack() as ctx:
        def sb(name, shape, dtype=F32):
            return ctx.enter_context(nc.sbuf_tensor(name, shape, dtype))

        def ps(name, shape):
            return ctx.enter_context(nc.psum_tensor(name, shape, F32))

        def sem(name):
            return ctx.enter_context(nc.semaphore(name))

        xs = sb("xs", [P, 2 * PAIR_SLOTS, 2, PIXELS])
        w1_sb = sb("w1_sb", [CHUNK, CHUNKS * QUARTERS, HIDDEN])
        w2_sb = sb("w2_sb", [HALF_HIDDEN, 2, PIXELS])
        consts = sb("consts", [P, table.shape[1]])
        count_consts = sb("count_consts", [P, count_table.shape[1]], U16)
        group_sums = sb("group_sums", [P, QUARTER])
        small = sb("small", [P, 22 + 33 + 32])
        row_sums = small[:, 0:1]
        minus_mean = small[:, 2:4]
        variance, inv_std = (small[:, c:c + 1] for c in range(4, 6))
        below = small[:, 6:7].bitcast(F16)[:, 0:1]
        candidate = small[:, 7:8].bitcast(I32)
        squares = small[:, 8:8 + PARTS]
        coef = small[:, 16:16 + QUARTERS]
        rank = small[:, 20:22]
        kept = small[:, 22:22 + 33].bitcast(I32)
        own_totals = small[:, 55:55 + 32]
        pixels = sb("pixels", [CHUNK, 2 * CHUNKS * QUARTERS + 30])
        hidden = sb("hidden", [HALF_HIDDEN, 2, 32])
        gate = sb("gate", [P, QUARTER])
        masked = sb("masked", [P, QUARTER])
        narrow = sb("narrow", [P, BANK], BF16)
        marks = sb("marks", [P, QUARTER + 2 * PIXELS // PARTS], U8)
        ties, unread = marks[:, 0:QUARTER], marks[:, QUARTER:]

        at = 0

        def part(n):
            nonlocal at
            at += n
            return consts[:, at - n:at]

        channel_to_rows, row_to_rows, row_to_channels = part(P), part(P), part(P)
        block_mask, less, exponent = part(QUARTERS), part(2), part(1)
        before, row_to_rows_16, own = (count_consts[:, a:b].bitcast(F16) for a, b in
                                       ((0, P), (P, P + 32), (P + 32, P + 64)))
        terms, weights = (count_consts[:, a:b].bitcast(BF16) for a, b in
                          ((P + 64, P + 72), (P + 72, P + 72 + 32 * STEPS)))
        turn = count_consts[:, P + 72 + 32 * STEPS:].bitcast(I32)

        sums_ps = ps("sums_ps", [P, 2, 512])
        net_ps = ps("net_ps", [P, 2, 512])
        stat_ps = ps("stat_ps", [P, 512])
        count_ps = ps("count_ps", [P, 512])
        spread_ps = ps("spread_ps", [P, 2, 512])
        mean_ps, mean8_ps, var_ps = stat_ps[:, 0:1], stat_ps[:, 1:2], stat_ps[:, 2:2 + PARTS]
        pixel_ps = stat_ps[0:CHUNK, 16:16 + CHUNKS * QUARTERS]
        parts_ps = net_ps[:, 0, 0:HIDDEN]
        hidden_ps = net_ps[0:HALF_HIDDEN, 1, 0:64]
        totals_ps, before_ps = count_ps[:, 0:32], count_ps[:, 32:33]

        const_in = sem("const_in")
        parts_sb = group_sums[:, 0:HIDDEN]

        w1_in = sem("w1_in")
        w2_in = sem("w2_in")
        loaded = [[sem(f"loaded_{i}_{h}") for h in range(2)] for i in range(2 * PAIR_SLOTS)]
        stored = [sem(f"stored_{i}") for i in range(2 * PAIR_SLOTS)]
        sums_made = sem("sums_made")
        sums_kept = sem("sums_kept")
        means_made = sem("means_made")
        means_kept = sem("means_kept")
        squared = sem("squared")
        var_made = sem("var_made")
        var_kept = sem("var_kept")
        inv_made = sem("inv_made")
        coef_made = sem("coef_made")
        pixels_made = sem("pixels_made")
        pixels_kept = sem("pixels_kept")
        parts_made = sem("parts_made")
        parts_kept = sem("parts_kept")
        hidden_made = sem("hidden_made")
        hidden_kept = sem("hidden_kept")
        logits_made = sem("logits_made")
        gate_made = sem("gate_made")
        counted = sem("counted")
        totalled = sem("totalled")
        dve_step = sem("dve_step")
        part_made = sem("part_made")
        rest_made = sem("rest_made")
        pad_made = sem("pad_made")
        masked_made = sem("masked_made")
        spread_made = sem("spread_made")
        added = sem("added")

        def upper(values):
            return values.bitcast(BF16).rearrange("p (n two) -> p n two", two=2)[:, :, 1]

        block = ctx.enter_context(nc.Block())

        def counter(pair):
            return lambda per, add=0: pair * per + add

        def each_pair(eng, first, body, last):
            first(0, 0, lambda d: d // PAIR_SLOTS + 1)
            rounds = (pairs - 3) // PAIR_SLOTS
            if rounds:
                with eng.Fori(0, rounds) as rounds_made:
                    for s in range(1, 1 + PAIR_SLOTS):
                        body(s % PAIR_SLOTS, rounds_made * PAIR_SLOTS + s,
                             lambda d, s=s: rounds_made + ((s + d) // PAIR_SLOTS + 1))
            for pair in range(rounds * PAIR_SLOTS + 1, pairs):
                step = body if pair < pairs - 1 else last
                step(pair % PAIR_SLOTS, pair, lambda d, pair=pair: (pair + d) // PAIR_SLOTS + 1)

        @block.sync
        def _(sp):
            sp.dma_start(consts[:], table).then_inc(const_in, 16)
            sp.dma_start(count_consts[:], count_table).then_inc(const_in, 16)

            def load(slot, n):
                for h in range(2):
                    cols = slice(h * CUT, (h + 1) * CUT)
                    sp.dma_start(xs[:, slot, :, cols], x_v[n, :, :, cols]).then_inc(loaded[slot][h], 16)

            for n in range(2 * PAIR_SLOTS):
                load(n, n)
                if n == 1:
                    sp.dma_start(w1_sb[:], w1).then_inc(w1_in, 16)
                    sp.dma_start(w2_sb[:], w2).then_inc(w2_in, 16)

            def image(slot, n, r, reload, r_before):
                for h in range(2):
                    cols = slice(h * CUT, (h + 1) * CUT)
                    sp.wait_ge(added, n * ADDS + (h + 1) * (ADDS // 2))
                    sp.dma_start(out_v[n, :, :, cols], xs[:, slot, :, cols]).then_inc(stored[slot], 16)
                    if h == 0 and reload:
                        last = (slot - 1) % (2 * PAIR_SLOTS)
                        sp.wait_ge(stored[last], (r_before + 1) * 32)
                        load(last, n - 1 + 2 * PAIR_SLOTS)

            slots = 2 * PAIR_SLOTS
            looped = max(0, (images + 1) // slots - 2)
            for n in range(slots):
                image(n, n, 0, n > 0 and n - 1 + slots < images, 0)
            if looped > 0:
                with sp.Fori(1, looped + 1) as r:
                    for slot in range(slots):
                        image(slot, r * slots + slot, r, True, r - (slot == 0))
            for n in range((looped + 1) * slots, images):
                image(n % slots, n, n // slots, n - 1 + slots < images, (n - 1) // slots)
            for slot in range(slots):
                sp.wait_ge(stored[slot], 32 * len(range(slot, images, slots)))

        @block.tensor
        def _(pe):
            t = nc.tensor

            def wide(column, m, k=P):
                return column.to_broadcast([k, m])

            def sums(s, pair, a, b, t2, use):
                n = pair * 2 + a
                if t2 == 0:
                    pe.wait_ge(loaded[2 * s + a][b], use * 16)
                    if b == 0:
                        pe.wait_ge(sums_kept, n)
                for q in range(QUARTERS):
                    lo = b * CUT + q * BANK
                    last = t.matmul(sums_ps[32 * q:32 * q + 32, b, 0:BANK], channel_to_rows[:, 0:32],
                                    xs[:, 2 * s + a, t2, lo:lo + BANK], start=t2 == 0, stop=t2 == 1)
                if b == 1 and t2 == 1:
                    last.then_inc(sums_made, 1)

            def means(pair, a):
                n = pair * 2 + a
                pe.wait_ge(sums_kept, n + 1)
                pe.wait_ge(pixels_kept, n)
                t.matmul(mean_ps, row_to_channels, row_sums, start=True, stop=True)
                t.matmul(mean8_ps, row_to_rows, row_sums, start=True, stop=True).then_inc(means_made, 1)

            def var(pair, a):
                pe.wait_ge(squared, (pair * 2 + a) * PARTS + PARTS)
                t.matmul(var_ps, channel_to_rows, squares, start=True, stop=True).then_inc(var_made, 1)

            def to_pixels(pair, a, ks=range(CHUNKS)):
                if ks[0] == 0:
                    pe.wait_ge(coef_made, pair * 2 + (a + 1))
                    t.matmul(pixel_ps, wide(minus_mean[:, 1:2], CHUNK),
                             coef.unsqueeze(1).to_broadcast([P, CHUNKS, QUARTERS]), start=True, stop=False)
                for k in ks:
                    last = t.matmul(pixel_ps[:, k * QUARTERS:(k + 1) * QUARTERS],
                                    group_sums[:, k * CHUNK:(k + 1) * CHUNK], coef,
                                    start=False, stop=k == CHUNKS - 1)
                if ks[-1] == CHUNKS - 1:
                    last.then_inc(pixels_made, 1)

            def first_layer(pair, ks):
                if ks[0] == 0:
                    pe.wait_ge(pixels_kept, pair * 2 + 2)
                    pe.wait_ge(gate_made, pair)
                for k in ks:
                    for q in range(QUARTERS):
                        c = k * QUARTERS + q
                        last = t.matmul(parts_ps[32 * q:32 * q + 32, :], pixels[:, 2 * c:2 * c + 32],
                                        w1_sb[:, c, :], start=k == 0, stop=k == CHUNKS - 1)
                if ks[-1] == CHUNKS - 1:
                    last.then_inc(parts_made, 1)

            def hidden_units(pair):
                pe.wait_ge(parts_kept, pair + 1)
                for u in range(2):
                    last = t.matmul(hidden_ps[:, 32 * u:32 * u + 32],
                                    parts_sb[:, u * HALF_HIDDEN:(u + 1) * HALF_HIDDEN],
                                    row_to_rows[:, 0:2].unsqueeze(1).to_broadcast([P, COPIES, 2]),
                                    start=True, stop=True)
                last.then_inc(hidden_made, 1)

            def second_layer(pair, b):
                if b == 0:
                    pe.wait_ge(hidden_kept, pair + 1)
                for u in range(2):
                    for q in range(QUARTERS):
                        lo = q * QUARTER + b * BANK
                        last = t.matmul(net_ps[32 * q:32 * q + 32, b, 0:BANK], hidden[:, u, :],
                                        w2_sb[:, u, lo:lo + BANK], start=u == 0, stop=u == 1)
                if b == 1:
                    last.then_inc(logits_made, 1)

            def totals(pair, k):
                pe.wait_ge(counted, pair * (STEPS + 1) + (k + 1))
                t.matmul(totals_ps, wide(below, P), row_to_rows_16, start=True, stop=True).then_inc(totalled, 1)

            def ties_before(pair):
                pe.wait_ge(counted, pair * (STEPS + 1) + (STEPS + 1))
                t.matmul(before_ps, before, below, start=True, stop=True).then_inc(totalled, 1)

            def spread(pair, a, c):
                if a == 0 and c == 0:
                    pe.wait_ge(masked_made, pair + 2)
                if a or c >= 2:
                    pe.wait_ge(added, pair * (2 * ADDS) + (a * ADDS + c - 1))
                q, b = divmod(c, 2)
                t.matmul(spread_ps[:, c % 2, 0:BANK], wide(terms[:, 2 * q + a:2 * q + a + 1], P),
                         upper(masked[:, b * BANK:(b + 1) * BANK]), start=True, stop=True).then_inc(spread_made, 1)

            def body(s, pair, uses, after=True):
                s1 = (s + 1) % PAIR_SLOTS
                nxt = pair + 1
                for k in range(STEPS):
                    totals(pair, k)
                    if after:
                        if k == 0:
                            means(nxt, 0)
                        if k < 4:
                            sums(s1, nxt, 1, k // 2, k % 2, uses(1))
                        if k == 4:
                            var(nxt, 0)
                        if k == 5:
                            to_pixels(nxt, 0, range(0, 2))
                        if k == 6:
                            to_pixels(nxt, 0, range(2, 4))
                        if k == 7:
                            to_pixels(nxt, 0, range(4, 7))
                ties_before(pair)
                if after:
                    means(nxt, 1)
                    after_next(s, pair, uses)
                for c in range(2 * ADDS):
                    spread(pair, c // ADDS, c % ADDS)
                    if after:
                        if c == 4:
                            var(nxt, 1)
                        if c == 6:
                            to_pixels(nxt, 1)
                        if 7 <= c < 11:
                            first_layer(nxt, range(2 * c - 14, min(2 * c - 12, CHUNKS)))
                        if c == 12:
                            hidden_units(nxt)
                        if c == 13:
                            second_layer(nxt, 0)
                        if c == 14:
                            second_layer(nxt, 1)

            def after_next(s, pair, uses):
                s2 = (s + 2) % PAIR_SLOTS
                if isinstance(pair, int) and pair + 2 >= pairs:
                    return
                for b in range(2):
                    for t2 in range(2):
                        sums(s2, pair + 2, 0, b, t2, uses(2))

            def first(s, pair, uses):
                pe.wait_ge(const_in, 32)
                for a in range(2):
                    for b in range(2):
                        for t2 in range(2):
                            sums(s, pair, a, b, t2, uses(0))
                    means(pair, a)
                    var(pair, a)
                    to_pixels(pair, a)
                pe.wait_ge(pad_made, 1)
                pe.wait_ge(w1_in, 16)
                pe.wait_ge(w2_in, 16)
                first_layer(pair, range(CHUNKS))
                hidden_units(pair)
                second_layer(pair, 0)
                second_layer(pair, 1)
                after_next(s - 1, pair - 1, lambda d: uses(d - 1))
                body(s, pair, uses)

            def last(s, pair, uses):
                body(s, pair, uses, after=False)

            each_pair(pe, first, body, last)

        @block.scalar
        def _(act):
            sc = nc.scalar
            sc.preload_act_table(ACT.Sigmoid)

            def split(pair, h, term):
                cols = slice(h * BANK, (h + 1) * BANK)
                if h == 1 and term == 0:
                    act.wait_ge(rest_made, pair * 4 + 2)
                if term == 1:
                    act.wait_ge(rest_made, pair * 4 + (2 * h + 1))
                sc.activation(narrow[:], upper((masked if term else gate)[:, cols]), ACT.Copy,
                              scale=less[:, term:term + 1]).then_inc(part_made, 1)

            def image_stats(s, pair, a, split_pair=None):
                slot, n = 2 * s + a, pair * 2 + a
                act.wait_ge(sums_made, n + 1)
                if a == 1:
                    act.wait_ge(pixels_made, n)
                sc.activation(group_sums[:].rearrange("p (b n) -> p b n", b=2), sums_ps[:, :, 0:BANK],
                              ACT.Copy, accum_out=row_sums).then_inc(sums_kept, 1)
                act.wait_ge(means_made, n + 1)
                sc.mul(minus_mean[:, 0:1], mean_ps, -1.0 / PER_GROUP)
                sc.mul(minus_mean[:, 1:2], mean8_ps, -8.0 / PER_GROUP).then_inc(means_kept, 1)
                act.wait_ge(means_kept, n + 1)
                flat = xs[:, slot].rearrange("p t n -> p (t n)")
                for j in range(PARTS):
                    if j:
                        act.wait_ge(squared, n * PARTS + j)
                    part = slice(j * 2 * PIXELS // PARTS, (j + 1) * 2 * PIXELS // PARTS)
                    sc.activation(unread, flat[:, part], ACT.Square,
                                  bias=minus_mean[:, 0:1], accum_out=squares[:, j:j + 1]).then_inc(squared, 1)
                    if split_pair is not None and j in (0, 2, 4, 6):
                        split(split_pair, j // 4, j // 2 % 2)
                act.wait_ge(var_made, n + 1)
                sc.activation(unread[:, 0:PARTS], var_ps, ACT.Copy, bias=EPS / PARTS, scale=1.0 / PER_GROUP,
                              accum_out=variance).then_inc(var_kept, 1)
                act.wait_ge(pixels_made, n + 1)
                sc.copy(pixels[:, 0:2 * CHUNKS * QUARTERS].rearrange("p (c a) -> p c a", a=2)[:, :, a],
                        pixel_ps).then_inc(pixels_kept, 1)

            def layers(pair):
                act.wait_ge(parts_made, pair + 1)
                sc.copy(parts_sb, parts_ps).then_inc(parts_kept, 1)
                act.wait_ge(hidden_made, pair + 1)
                sc.activation(hidden[:].rearrange("p u m -> p (u m)"), hidden_ps, ACT.Relu).then_inc(hidden_kept, 1)
                act.wait_ge(logits_made, pair + 1)
                act.wait_ge(masked_made, pair + 1)
                sc.activation(gate[:].rearrange("p (b n) -> p b n", b=2), net_ps[:, :, 0:BANK],
                              ACT.Sigmoid).then_inc(gate_made, 1)
                act.wait_ge(gate_made, pair + 1)

            def body(s, pair, uses):
                image_stats((s + 1) % PAIR_SLOTS, pair + 1, 0, split_pair=pair)
                image_stats((s + 1) % PAIR_SLOTS, pair + 1, 1)
                layers(pair + 1)

            def first(s, pair, uses):
                image_stats(s, pair, 0)
                image_stats(s, pair, 1)
                layers(pair)
                body(s, pair, uses)

            def last(s, pair, uses):
                for h in range(2):
                    for term in range(2):
                        split(pair, h, term)

            each_pair(act, first, body, last)

        @block.gpsimd
        def _(pool):
            nc.gpsimd.memset(pixels[:, 2 * CHUNKS * QUARTERS:], 0.0).then_inc(pad_made, 1)
            pool.wait_ge(const_in, 32)

            def coefficients(n):
                pool.wait_ge(var_kept, n + 1)
                nc.gpsimd.tensor_tensor(inv_std, variance, exponent, ALU.pow).then_inc(inv_made, 1)
                pool.wait_ge(inv_made, n + 1)
                if not (isinstance(n, int) and n == 0):
                    pool.wait_ge(pixels_made, n)
                nc.gpsimd.tensor_tensor(coef, block_mask, inv_std.to_broadcast([P, QUARTERS]),
                                        ALU.mult).then_inc(coef_made, 1)

            def split(pair):
                for h in range(2):
                    cols = slice(h * BANK, (h + 1) * BANK)
                    for term in range(2):
                        pool.wait_ge(part_made, pair * 4 + (2 * h + term + 1))
                        if h == 0 and term == 0 and not (isinstance(pair, int) and pair == 0):
                            pool.wait_ge(spread_made, pair * (2 * ADDS))
                        nc.gpsimd.tensor_tensor(masked[:, cols], (masked if term else gate)[:, cols], narrow[:],
                                                ALU.add).then_inc(rest_made, 1)

            def body(s, pair, uses):
                split(pair)
                coefficients(pair * 2 + 2)
                coefficients(pair * 2 + 3)

            def first(s, pair, uses):
                coefficients(0)
                coefficients(1)
                body(s, pair, uses)

            each_pair(pool, first, body, lambda s, pair, uses: split(pair))

        @block.vector
        def _(dve):
            v = nc.vector
            dve.wait_ge(const_in, 32)
            dve.sem_inc(masked_made, 1)
            CHAIN = 2 * STEPS + 9

            def add(s, pair, a, c):
                dve.wait_ge(spread_made, pair * (2 * ADDS) + (a * ADDS + c + 1))
                piece = xs[:, 2 * s + a, :, c * BANK:(c + 1) * BANK]
                v.tensor_tensor(piece, piece, spread_ps[:, c % 2, 0:BANK].unsqueeze(1).to_broadcast([P, 2, BANK]),
                                ALU.add).then_inc(added, 1)

            def body(s, pair, uses):
                i = counter(pair)
                done = [0]

                def step(instruction):
                    done[0] += 1
                    instruction.then_inc(dve_step, 1)
                    dve.wait_ge(dve_step, i(CHAIN, done[0]))

                step(v.tensor_copy(candidate, turn[:, 0:1]))
                dve.wait_ge(gate_made, i(1, 1))
                value = small[:, 7:8]
                for k in range(STEPS):
                    v.tensor_scalar(ties, gate[:], value, None, ALU.is_lt, ALU.add,
                                    accum_out=below).then_inc(counted, 1)
                    v.tensor_tensor(kept[:, 32:33], candidate, turn[:, k + 1:k + 2] if k + 1 < STEPS else
                                    turn[:, STEPS:STEPS + 1], ALU.bitwise_xor)
                    dve.wait_ge(totalled, i(STEPS + 1, k + 1))
                    if k == STEPS - 1:
                        v.tensor_tensor(own_totals, totals_ps, own, ALU.mult)
                    step(v.scalar_tensor_tensor(kept[:, 0:32], totals_ps, CUT - 0.5, weights[:, 32 * k:32 * k + 32],
                                                ALU.is_lt, ALU.mult))
                    step(v.tensor_reduce(candidate, kept, AX.X, ALU.bitwise_xor))
                v.tensor_scalar(ties, gate[:], value, None, ALU.is_equal, ALU.add,
                                accum_out=below).then_inc(counted, 1)
                step(v.scalar_tensor_tensor(own_totals, own_totals, CUT - 0.5, own_totals,
                                            ALU.is_lt, ALU.mult))
                step(v.tensor_reduce(rank[:, 0:1], own_totals, AX.X, ALU.max))
                dve.wait_ge(totalled, i(STEPS + 1, STEPS + 1))
                step(v.tensor_tensor(rank[:, 1:2], rank[:, 0:1], before_ps, ALU.add))
                ranks = narrow[:].bitcast(I16)
                for h in range(2):
                    cols = slice(h * BANK, (h + 1) * BANK)
                    if h == 0:
                        dve.wait_ge(rest_made, i(4, 4))
                    step(v.tensor_tensor_scan(ranks, ties[:, cols], ties[:, cols], rank[:, 1:2], ALU.add, ALU.max))
                    if h == 0:
                        v.tensor_copy(rank[:, 1:2], ranks[:, BANK - 1:BANK])
                    step(v.scalar_tensor_tensor(ties[:, cols], ranks, CUT + 0.5, ties[:, cols], ALU.is_gt, ALU.mult))
                step(v.scalar_tensor_tensor(ties, gate[:], value, ties, ALU.is_gt, ALU.max))
                v.tensor_tensor(masked[:], masked[:], ties, ALU.mult).then_inc(masked_made, 1)
                assert done[0] == CHAIN, done
                for a in range(2):
                    for c in range(ADDS):
                        add(s, pair, a, c)

            each_pair(dve, body, body, body)


def kernel(x, L0_conv_W1, L0_conv_W2):
    import concourse.bacc as bacc
    from concourse.bass_utils import run_bass_kernel_spmd

    w1 = np.asarray(L0_conv_W1).reshape(HIDDEN, 2, QUARTERS, BANK).transpose(0, 2, 1, 3)
    w1 = w1.reshape(HIDDEN, QUARTERS, CHUNKS, CHUNK).transpose(3, 2, 1, 0)
    w1 = np.ascontiguousarray(w1.reshape(CHUNK, CHUNKS * QUARTERS, HIDDEN))
    w2 = np.asarray(L0_conv_W2).T.reshape(2, HALF_HIDDEN, PIXELS).transpose(1, 0, 2)
    table, count_table = constants()
    arrays = {"x": np.ascontiguousarray(x), "w1": w1, "w2": np.ascontiguousarray(w2),
              "table": table, "count_table": count_table}

    nc = bacc.Bacc("TRN2", target_bir_lowering=False, num_devices=1)
    ins = [nc.dram_tensor(k, a.shape, mybir.dt.from_np(a.dtype), kind="ExternalInput").ap() for k, a in arrays.items()]
    out = nc.dram_tensor("out", arrays["x"].shape, F32, kind="ExternalOutput").ap()
    gate_kernel(nc, *ins, out)
    result = run_bass_kernel_spmd(nc, [arrays], core_ids=[0])
    return result.results[0]["out"]
```

```python
from contextlib import ExitStack

import numpy as np

import concourse.bass as bass
from concourse import mybir

F32, F16, BF16 = mybir.dt.float32, mybir.dt.float16, mybir.dt.bfloat16
I32, I16, U16, U8 = mybir.dt.int32, mybir.dt.int16, mybir.dt.uint16, mybir.dt.uint8
ALU, ACT, AX = mybir.AluOpType, mybir.ActivationFunctionType, mybir.AxisListType

P = 128
CHANNELS, PIXELS, GROUPS, HIDDEN = 256, 56 * 56, 32, 196
CUT = PIXELS // 2
EPS = 1e-5
PAIR_SLOTS = 3
QUARTERS, COPIES = 4, 16
QUARTER = PIXELS // QUARTERS
BANK = QUARTER // 2
CHUNK = 112
CHUNKS = QUARTER // CHUNK
HALF_HIDDEN = HIDDEN // 2
PER_GROUP = (CHANNELS // GROUPS) * PIXELS
BITS, STEPS = 4, 8
PARTS = 8
SPREADS = 3
ADDS = 2 * QUARTERS


def constants():
    p = np.arange(P)
    quarter, copy, image = p // 32, p % 32 // 2, p % 2
    channel_to_rows = (p[:, None] // 4 == p % 32).astype(np.float32)
    row_to_rows = (p[:, None] % 32 == p % 32).astype(np.float32)
    row_to_channels = (p[:, None] % 32 == p // 4).astype(np.float32)
    own = (image[:, None] == np.arange(32) % 2).astype(np.float32)
    before = ((image[:, None] == image) & (quarter[:, None] < quarter) & (copy[:, None] == 0)).astype(np.float32)
    block = (quarter[:, None] == np.arange(QUARTERS)).astype(np.float32) / CHANNELS
    terms = (p[:, None] // 32 == np.arange(8) // 2) & (p[:, None] % 2 == np.arange(8) % 2) & (p[:, None] % 32 < 6)
    less = -np.stack([copy >= 1, copy >= 2], 1).astype(np.float32)
    exponent = np.full((P, 1), -0.5, np.float32)
    number = np.arange(32) // 2
    shifts = [BITS * (STEPS - 1 - k) for k in range(STEPS)]
    top = 4
    weights = np.zeros((P, STEPS, 32), np.float32)
    bits = np.zeros((P, STEPS + 1), np.int32)
    for k, shift in enumerate(shifts):
        valid = (number > 0) & ((number < top) | (k > 0))
        weights[:, k] = own * np.where(valid, (number ^ (number - 1)) << shift, 0)
        bits[:, k] = np.where((copy < top) | (k > 0), copy, 0).astype(np.int64) << shift
    turns = np.concatenate([bits[:, :1], bits[:, :-1] ^ bits[:, 1:]], 1).astype(np.int32)
    table = np.concatenate([channel_to_rows, row_to_rows, row_to_channels, block, less, exponent], 1)
    halves = np.concatenate([before, row_to_rows[:, 0:32], own], 1).astype(np.float16).view(np.uint16)
    wide_range = np.concatenate([terms.astype(np.float32), weights.reshape(P, -1)], 1)
    wide_range = (wide_range.view(np.uint32) >> 16).astype(np.uint16)
    return table, np.concatenate([halves, wide_range, turns.view(np.uint16)], 1)


def gate_kernel(nc, x, w1, w2, table, count_table, out):
    images = x.shape[0]
    pairs = images // 2
    x_v = x.rearrange("n (p t) h w -> n p t (h w)", p=P)
    out_v = out.rearrange("n (p t) h w -> n p t (h w)", p=P)

    with ExitStack() as ctx:
        def sb(name, shape, dtype=F32):
            return ctx.enter_context(nc.sbuf_tensor(name, shape, dtype))

        def ps(name, shape):
            return ctx.enter_context(nc.psum_tensor(name, shape, F32))

        def sem(name):
            return ctx.enter_context(nc.semaphore(name))

        xs = sb("xs", [P, 2 * PAIR_SLOTS, 2, PIXELS])
        w1_sb = sb("w1_sb", [CHUNK, CHUNKS * QUARTERS, HIDDEN])
        w2_sb = sb("w2_sb", [HALF_HIDDEN, 2, PIXELS])
        consts = sb("consts", [P, table.shape[1]])
        count_consts = sb("count_consts", [P, count_table.shape[1]], U16)
        group_sums = sb("group_sums", [P, QUARTER])
        narrow = sb("narrow", [P, BANK], BF16)
        small = sb("small", [P, 22 + 33 + 32])
        row_sums = small[:, 0:1]
        minus_mean = small[:, 2:4]
        variance, inv_std = (small[:, c:c + 1] for c in range(4, 6))
        below = small[:, 6:7].bitcast(F16)[:, 0:1]
        candidate = small[:, 7:8].bitcast(I32)
        squares = small[:, 8:8 + PARTS]
        coef = small[:, 16:16 + QUARTERS]
        rank = small[:, 20:22]
        parts_sb = narrow[:].bitcast(F32)
        kept = small[:, 22:22 + 33].bitcast(I32)
        own_totals = small[:, 55:55 + 32]
        pixels = sb("pixels", [CHUNK, 2 * CHUNKS * QUARTERS + 30])
        hidden = sb("hidden", [HALF_HIDDEN, 2, 32])
        gate = sb("gate", [P, QUARTER])
        masked = sb("masked", [P, QUARTER])
        marks = sb("marks", [P, QUARTER + 2 * PIXELS // PARTS], U8)
        ties, unread = marks[:, 0:QUARTER], marks[:, QUARTER:]

        at = 0

        def part(n):
            nonlocal at
            at += n
            return consts[:, at - n:at]

        channel_to_rows, row_to_rows, row_to_channels = part(P), part(P), part(P)
        block_mask, less, exponent = part(QUARTERS), part(2), part(1)
        before, row_to_rows_16, own = (count_consts[:, a:b].bitcast(F16) for a, b in
                                       ((0, P), (P, P + 32), (P + 32, P + 64)))
        terms, weights = (count_consts[:, a:b].bitcast(BF16) for a, b in
                          ((P + 64, P + 72), (P + 72, P + 72 + 32 * STEPS)))
        turn = count_consts[:, P + 72 + 32 * STEPS:].bitcast(I32)

        sums_ps = ps("sums_ps", [P, 2, 512])
        net_ps = ps("net_ps", [P, 2, 512])
        stat_ps = ps("stat_ps", [P, 512])
        count_ps = ps("count_ps", [P, 512])
        spread_ps = [ps("spread_ps_0", [P, 512]), ps("spread_ps_1", [P, 512]), count_ps]
        mean_ps, mean8_ps, var_ps = stat_ps[:, 0:1], stat_ps[:, 1:2], stat_ps[:, 2:2 + PARTS]
        pixel_ps = stat_ps[0:CHUNK, 16:16 + CHUNKS * QUARTERS]
        parts_ps = net_ps[:, 0, 0:HIDDEN]
        hidden_ps = net_ps[0:HALF_HIDDEN, 1, 0:64]
        totals_ps, before_ps = count_ps[:, 0:32], count_ps[:, 32:33]

        const_in = sem("const_in")
        w1_in = sem("w1_in")
        w2_in = sem("w2_in")
        loaded = [[sem(f"loaded_{i}_{h}") for h in range(2)] for i in range(2 * PAIR_SLOTS)]
        stored = [[sem(f"stored_{i}_{h}") for h in range(2)] for i in range(2 * PAIR_SLOTS)]
        sums_made = sem("sums_made")
        sums_kept = sem("sums_kept")
        means_made = sem("means_made")
        means_kept = sem("means_kept")
        squared = sem("squared")
        var_made = sem("var_made")
        var_kept = sem("var_kept")
        inv_made = sem("inv_made")
        coef_made = sem("coef_made")
        pixels_made = sem("pixels_made")
        pixels_kept = sem("pixels_kept")
        parts_made = sem("parts_made")
        parts_kept = sem("parts_kept")
        hidden_made = sem("hidden_made")
        hidden_kept = sem("hidden_kept")
        logits_made = sem("logits_made")
        gate_made = sem("gate_made")
        counted = sem("counted")
        totalled = sem("totalled")
        dve_step = sem("dve_step")
        part_made = sem("part_made")
        rest_made = sem("rest_made")
        pad_made = sem("pad_made")
        half_masked = sem("half_masked")
        masked_made = sem("masked_made")
        spread_made = sem("spread_made")
        added = sem("added")

        def upper(values):
            return values.bitcast(BF16).rearrange("p (n two) -> p n two", two=2)[:, :, 1]

        block = ctx.enter_context(nc.Block())

        def counter(pair):
            return lambda per, add=0: pair * per + add

        def each_pair(eng, first, body, last):
            first(0, 0, lambda d: d // PAIR_SLOTS + 1)
            rounds = (pairs - 1) // PAIR_SLOTS - 1
            if rounds:
                with eng.Fori(0, rounds) as rounds_made:
                    for s in range(1, 1 + PAIR_SLOTS):
                        body(s % PAIR_SLOTS, rounds_made * PAIR_SLOTS + s,
                             lambda d, s=s: rounds_made + ((s + d) // PAIR_SLOTS + 1))
            for pair in range(rounds * PAIR_SLOTS + 1, pairs):
                step = body if pair < pairs - 1 else last
                step(pair % PAIR_SLOTS, pair, lambda d, pair=pair: (pair + d) // PAIR_SLOTS + 1)

        @block.sync
        def _(sp):
            sp.dma_start(consts[:], table).then_inc(const_in, 16)
            sp.dma_start(count_consts[:], count_table).then_inc(const_in, 16)

            def load(slot, n, h):
                cols = slice(h * CUT, (h + 1) * CUT)
                sp.dma_start(xs[:, slot, :, cols], x_v[n, :, :, cols]).then_inc(loaded[slot][h], 16)

            for n in range(2 * PAIR_SLOTS):
                load(n, n, 0)
                load(n, n, 1)
                if n == 2:
                    sp.dma_start(w1_sb[:], w1).then_inc(w1_in, 16)
                    sp.dma_start(w2_sb[:], w2).then_inc(w2_in, 16)

            def body(s, pair, uses):
                def store(a, h, first, last):
                    sp.wait_ge(added, (pair * 2 + a) * ADDS + last + 1)
                    cols = slice(first * BANK, (last + 1) * BANK)
                    sp.dma_start(out_v[pair * 2 + a, :, :, cols],
                                 xs[:, 2 * s + a, :, cols]).then_inc(stored[2 * s + a][h], 16)

                def load_anew(a, h, stores):
                    if not (isinstance(pair, int) and pair + PAIR_SLOTS >= pairs):
                        sp.wait_ge(stored[2 * s + a][h], uses(0) * (16 * stores))
                        load(2 * s + a, (pair + PAIR_SLOTS) * 2 + a, h)

                store(0, 0, 0, 1)
                store(0, 0, 2, 3)
                store(0, 1, 4, 5)
                store(0, 1, 6, 7)
                load_anew(0, 0, 2)
                load_anew(0, 1, 2)
                store(1, 0, 0, 3)
                store(1, 1, 4, 7)
                load_anew(1, 0, 1)
                load_anew(1, 1, 1)

            each_pair(sp, body, body, body)
            for slot in range(2 * PAIR_SLOTS):
                for h in range(2):
                    uses_made = len(range(slot // 2, pairs, PAIR_SLOTS))
                    sp.wait_ge(stored[slot][h], uses_made * (32 if slot % 2 == 0 else 16))

        @block.tensor
        def _(pe):
            t = nc.tensor

            def wide(column, m, k=P):
                return column.to_broadcast([k, m])

            def sums(s, pair, a, b, t2, use):
                n = pair * 2 + a
                if t2 == 0:
                    pe.wait_ge(loaded[2 * s + a][b], use * 16)
                    if b == 0:
                        pe.wait_ge(sums_kept, n)
                for q in range(QUARTERS):
                    lo = b * CUT + q * BANK
                    last = t.matmul(sums_ps[32 * q:32 * q + 32, b, 0:BANK], channel_to_rows[:, 0:32],
                                    xs[:, 2 * s + a, t2, lo:lo + BANK], start=t2 == 0, stop=t2 == 1)
                if b == 1 and t2 == 1:
                    last.then_inc(sums_made, 1)

            def means(pair, a):
                n = pair * 2 + a
                pe.wait_ge(sums_kept, n + 1)
                pe.wait_ge(pixels_kept, n)
                t.matmul(mean_ps, row_to_channels, row_sums, start=True, stop=True)
                t.matmul(mean8_ps, row_to_rows, row_sums, start=True, stop=True).then_inc(means_made, 1)

            def var(pair, a):
                pe.wait_ge(squared, (pair * 2 + a) * PARTS + PARTS)
                t.matmul(var_ps, channel_to_rows, squares, start=True, stop=True).then_inc(var_made, 1)

            def to_pixels(pair, a, ks=range(CHUNKS)):
                if ks[0] == 0:
                    pe.wait_ge(coef_made, pair * 2 + (a + 1))
                    t.matmul(pixel_ps, wide(minus_mean[:, 1:2], CHUNK),
                             coef.unsqueeze(1).to_broadcast([P, CHUNKS, QUARTERS]), start=True, stop=False)
                for k in ks:
                    last = t.matmul(pixel_ps[:, k * QUARTERS:(k + 1) * QUARTERS],
                                    group_sums[:, k * CHUNK:(k + 1) * CHUNK], coef,
                                    start=False, stop=k == CHUNKS - 1)
                if ks[-1] == CHUNKS - 1:
                    last.then_inc(pixels_made, 1)

            def first_layer(pair, ks):
                if ks[0] == 0:
                    pe.wait_ge(pixels_kept, pair * 2 + 2)
                    pe.wait_ge(gate_made, pair)
                for k in ks:
                    for q in range(QUARTERS):
                        c = k * QUARTERS + q
                        last = t.matmul(parts_ps[32 * q:32 * q + 32, :], pixels[:, 2 * c:2 * c + 32],
                                        w1_sb[:, c, :], start=k == 0, stop=k == CHUNKS - 1)
                if ks[-1] == CHUNKS - 1:
                    last.then_inc(parts_made, 1)

            def hidden_units(pair):
                pe.wait_ge(parts_kept, pair + 1)
                for u in range(2):
                    last = t.matmul(hidden_ps[:, 32 * u:32 * u + 32],
                                    parts_sb[:, u * HALF_HIDDEN:(u + 1) * HALF_HIDDEN],
                                    row_to_rows[:, 0:2].unsqueeze(1).to_broadcast([P, COPIES, 2]),
                                    start=True, stop=True)
                last.then_inc(hidden_made, 1)

            def second_layer(pair, b, u):
                if b == 0 and u == 0:
                    pe.wait_ge(hidden_kept, pair + 1)
                for q in range(QUARTERS):
                    lo = q * QUARTER + b * BANK
                    last = t.matmul(net_ps[32 * q:32 * q + 32, b, 0:BANK], hidden[:, u, :],
                                    w2_sb[:, u, lo:lo + BANK], start=u == 0, stop=u == 1)
                if b == 1 and u == 1:
                    last.then_inc(logits_made, 1)

            def totals(pair, k):
                pe.wait_ge(counted, pair * (STEPS + 1) + (k + 1))
                t.matmul(totals_ps, wide(below, P), row_to_rows_16, start=True, stop=True).then_inc(totalled, 1)

            def ties_before(pair):
                pe.wait_ge(counted, pair * (STEPS + 1) + (STEPS + 1))
                t.matmul(before_ps, before, below, start=True, stop=True).then_inc(totalled, 1)

            def spread(pair, i):
                a, c = divmod(i, ADDS)
                if i == 0:
                    pe.wait_ge(half_masked, pair + 1)
                if i == 1:
                    pe.wait_ge(masked_made, pair + 2)
                if i >= SPREADS:
                    pe.wait_ge(added, pair * (2 * ADDS) + (i - SPREADS + 1))
                q, b = divmod(c, 2)
                t.matmul(spread_ps[i % SPREADS][:, 0:BANK], wide(terms[:, 2 * q + a:2 * q + a + 1], P),
                         upper(masked[:, b * BANK:(b + 1) * BANK]), start=True, stop=True).then_inc(spread_made, 1)

            def body(s, pair, uses, after=True):
                nxt = pair + 1
                s2, far = (s + 2) % PAIR_SLOTS, pair + 2
                after_next = not (isinstance(pair, int) and far >= pairs)

                def during_search(k):
                    if k == 0:
                        var(nxt, 1)
                    if k == 1:
                        to_pixels(nxt, 1, range(0, 2))
                    if k == 2:
                        to_pixels(nxt, 1, range(2, 7))
                    if k == 3:
                        first_layer(nxt, range(0, 2))
                    if k == 4:
                        first_layer(nxt, range(2, 3))
                        if after_next:
                            sums(s2, far, 0, 0, 0, uses(2))
                    if k == 5:
                        if after_next:
                            sums(s2, far, 0, 0, 1, uses(2))
                            sums(s2, far, 0, 1, 0, uses(2))
                    if k == 6:
                        first_layer(nxt, range(3, 5))
                        if after_next:
                            sums(s2, far, 0, 1, 1, uses(2))
                    if k == 7:
                        first_layer(nxt, range(5, 7))
                        if after_next:
                            means(far, 0)
                    if k == 8:
                        hidden_units(nxt)
                        second_layer(nxt, 0, 0)
                        second_layer(nxt, 0, 1)
                        second_layer(nxt, 1, 0)

                def during_adds(c):
                    if c == 1:
                        if after_next:
                            sums(s2, far, 1, 0, 0, uses(2))
                    if c == 2:
                        if after_next:
                            sums(s2, far, 1, 0, 1, uses(2))
                    if c == 3:
                        if after_next:
                            var(far, 0)
                    if c == 4:
                        if after_next:
                            sums(s2, far, 1, 1, 0, uses(2))
                            sums(s2, far, 1, 1, 1, uses(2))
                    if c == 5:
                        if after_next:
                            to_pixels(far, 0, range(0, 2))
                    if c == 6:
                        if after_next:
                            to_pixels(far, 0, range(2, 7))
                    if c == 8:
                        second_layer(nxt, 1, 1)
                    if c == 9:
                        if after_next:
                            means(far, 1)

                for k in range(STEPS + 1):
                    if k < STEPS:
                        totals(pair, k)
                    else:
                        ties_before(pair)
                    if after:
                        during_search(k)
                for c in range(2 * ADDS):
                    spread(pair, c)
                    if after:
                        during_adds(c)

            def first(s, pair, uses):
                pe.wait_ge(const_in, 32)

                def all_sums(s, pair, a):
                    for b in range(2):
                        for t2 in range(2):
                            sums(s, pair, a, b, t2, 1)

                all_sums(s, pair, 0)
                for a in range(2):
                    means(pair, a)
                    all_sums(s + a, pair + a, 1 - a)
                    var(pair, a)
                    to_pixels(pair, a)
                means(pair + 1, 0)
                pe.wait_ge(pad_made, 1)
                pe.wait_ge(w1_in, 16)
                pe.wait_ge(w2_in, 16)
                first_layer(pair, range(CHUNKS))
                hidden_units(pair)
                for part in range(4):
                    second_layer(pair, part // 2, part % 2)
                all_sums(s + 1, pair + 1, 1)
                var(pair + 1, 0)
                to_pixels(pair + 1, 0)
                means(pair + 1, 1)
                body(s, pair, uses)

            def last(s, pair, uses):
                body(s, pair, uses, after=False)

            each_pair(pe, first, body, last)

        @block.scalar
        def _(act):
            sc = nc.scalar
            sc.preload_act_table(ACT.Sigmoid)

            def split(pair, h, term):
                cols = slice(h * BANK, (h + 1) * BANK)
                if h == 1 and term == 0:
                    act.wait_ge(rest_made, pair * 4 + 2)
                if term == 1:
                    act.wait_ge(rest_made, pair * 4 + (2 * h + 1))
                sc.activation(narrow[:], upper((masked if term else gate)[:, cols]), ACT.Copy,
                              scale=less[:, term:term + 1]).then_inc(part_made, 1)

            def means(pair, a):
                n = pair * 2 + a
                act.wait_ge(sums_made, n + 1)
                if not (isinstance(n, int) and n == 0):
                    act.wait_ge(pixels_made, n)
                sc.activation(group_sums[:].rearrange("p (b n) -> p b n", b=2), sums_ps[:, :, 0:BANK],
                              ACT.Copy, accum_out=row_sums).then_inc(sums_kept, 1)
                act.wait_ge(means_made, n + 1)
                sc.mul(minus_mean[:, 0:1], mean_ps, -1.0 / PER_GROUP)
                sc.mul(minus_mean[:, 1:2], mean8_ps, -8.0 / PER_GROUP).then_inc(means_kept, 1)

            def square(s, pair, a, js):
                n = pair * 2 + a
                flat = xs[:, 2 * s + a].rearrange("p t n -> p (t n)")
                if 0 in js:
                    act.wait_ge(means_kept, n + 1)
                for j in js:
                    if j:
                        act.wait_ge(squared, n * PARTS + j)
                    part = slice(j * 2 * PIXELS // PARTS, (j + 1) * 2 * PIXELS // PARTS)
                    sc.activation(unread, flat[:, part], ACT.Square,
                                  bias=minus_mean[:, 0:1], accum_out=squares[:, j:j + 1]).then_inc(squared, 1)

            def variance_of(pair, a):
                act.wait_ge(var_made, pair * 2 + (a + 1))
                sc.activation(unread[:, 0:PARTS], var_ps, ACT.Copy, bias=EPS / PARTS, scale=1.0 / PER_GROUP,
                              accum_out=variance).then_inc(var_kept, 1)

            def keep_pixels(pair, a):
                act.wait_ge(pixels_made, pair * 2 + (a + 1))
                sc.copy(pixels[:, 0:2 * CHUNKS * QUARTERS].rearrange("p (c a) -> p c a", a=2)[:, :, a],
                        pixel_ps).then_inc(pixels_kept, 1)

            def layers(s, pair):
                nxt = pair + 1
                after = not (isinstance(pair, int) and nxt >= pairs)
                if after:
                    means(nxt, 0)
                act.wait_ge(parts_made, pair + 1)
                if not (isinstance(pair, int) and pair == 0):
                    act.wait_ge(rest_made, pair * 4)
                sc.copy(parts_sb, parts_ps).then_inc(parts_kept, 1)
                if after:
                    square(s, nxt, 0, range(0, 1))
                act.wait_ge(hidden_made, pair + 1)
                sc.activation(hidden[:].rearrange("p u m -> p (u m)"), hidden_ps, ACT.Relu).then_inc(hidden_kept, 1)
                if after:
                    square(s, nxt, 0, range(1, PARTS))
                    variance_of(nxt, 0)
                    if not (isinstance(pair, int) and pair == 0):
                        keep_pixels(nxt, 0)
                        means(nxt, 1)
                        square(s, nxt, 1, range(0, 5))
                act.wait_ge(logits_made, pair + 1)
                act.wait_ge(masked_made, pair + 1)
                sc.activation(gate[:].rearrange("p (b n) -> p b n", b=2), net_ps[:, :, 0:BANK],
                              ACT.Sigmoid).then_inc(gate_made, 1)
                if after:
                    if isinstance(pair, int) and pair == 0:
                        keep_pixels(nxt, 0)
                        means(nxt, 1)
                        square(s, nxt, 1, range(PARTS))
                    else:
                        square(s, nxt, 1, range(5, PARTS))
                act.wait_ge(gate_made, pair + 1)

            def body(s, pair, uses):
                nxt = pair + 1
                variance_of(nxt, 1)
                split(pair, 0, 0)
                keep_pixels(nxt, 1)
                split(pair, 0, 1)
                split(pair, 1, 0)
                split(pair, 1, 1)
                layers((s + 2) % PAIR_SLOTS, nxt)

            def first(s, pair, uses):
                for a in range(2):
                    means(pair, a)
                    square(s, pair, a, range(PARTS))
                    variance_of(pair, a)
                    keep_pixels(pair, a)
                layers(s + 1, pair)
                body(s, pair, uses)

            def last(s, pair, uses):
                for h in range(2):
                    for term in range(2):
                        split(pair, h, term)

            each_pair(act, first, body, last)

        @block.gpsimd
        def _(pool):
            nc.gpsimd.memset(pixels[:, 2 * CHUNKS * QUARTERS:], 0.0).then_inc(pad_made, 1)
            pool.wait_ge(const_in, 32)

            def coefficients(n):
                pool.wait_ge(var_kept, n + 1)
                nc.gpsimd.tensor_tensor(inv_std, variance, exponent, ALU.pow).then_inc(inv_made, 1)
                pool.wait_ge(inv_made, n + 1)
                if not (isinstance(n, int) and n == 0):
                    pool.wait_ge(pixels_made, n)
                nc.gpsimd.tensor_tensor(coef, block_mask, inv_std.to_broadcast([P, QUARTERS]),
                                        ALU.mult).then_inc(coef_made, 1)

            def split(pair):
                for h in range(2):
                    cols = slice(h * BANK, (h + 1) * BANK)
                    for term in range(2):
                        pool.wait_ge(part_made, pair * 4 + (2 * h + term + 1))
                        if h == 0 and term == 0 and not (isinstance(pair, int) and pair == 0):
                            pool.wait_ge(spread_made, pair * (2 * ADDS))
                        nc.gpsimd.tensor_tensor(masked[:, cols], (masked if term else gate)[:, cols], narrow[:],
                                                ALU.add).then_inc(rest_made, 1)

            def body(s, pair, uses):
                coefficients(pair * 2 + 3)
                split(pair)
                if not (isinstance(pair, int) and pair + 2 >= pairs):
                    coefficients(pair * 2 + 4)

            def first(s, pair, uses):
                coefficients(0)
                coefficients(1)
                coefficients(2)
                body(s, pair, uses)

            each_pair(pool, first, body, lambda s, pair, uses: split(pair))

        @block.vector
        def _(dve):
            v = nc.vector
            dve.wait_ge(const_in, 32)
            dve.sem_inc(masked_made, 1)
            CHAIN = 2 * STEPS + 10

            def body(s, pair, uses):
                i = counter(pair)
                done = [0]

                def mark(instruction):
                    done[0] += 1
                    instruction.then_inc(dve_step, 1)
                    return done[0]

                def wait_for(marked):
                    dve.wait_ge(dve_step, i(CHAIN, marked))

                def step(instruction):
                    wait_for(mark(instruction))

                step(v.tensor_copy(candidate, turn[:, 0:1]))
                dve.wait_ge(gate_made, i(1, 1))
                value = small[:, 7:8]
                for k in range(STEPS):
                    v.tensor_scalar(ties, gate[:], value, None, ALU.is_lt, ALU.add,
                                    accum_out=below).then_inc(counted, 1)
                    v.tensor_tensor(kept[:, 32:33], candidate, turn[:, k + 1:k + 2] if k + 1 < STEPS else
                                    turn[:, STEPS:STEPS + 1], ALU.bitwise_xor)
                    dve.wait_ge(totalled, i(STEPS + 1, k + 1))
                    weighed = mark(v.scalar_tensor_tensor(kept[:, 0:32], totals_ps, CUT - 0.5,
                                                          weights[:, 32 * k:32 * k + 32], ALU.is_lt, ALU.mult))
                    if k == STEPS - 1:
                        v.tensor_tensor(own_totals, totals_ps, own, ALU.mult)
                    wait_for(weighed)
                    step(v.tensor_reduce(candidate, kept, AX.X, ALU.bitwise_xor))
                v.tensor_scalar(ties, gate[:], value, None, ALU.is_equal, ALU.add,
                                accum_out=below).then_inc(counted, 1)
                step(v.scalar_tensor_tensor(own_totals, own_totals, CUT - 0.5, own_totals,
                                            ALU.is_lt, ALU.mult))
                step(v.tensor_reduce(rank[:, 0:1], own_totals, AX.X, ALU.max))
                dve.wait_ge(totalled, i(STEPS + 1, STEPS + 1))
                step(v.tensor_tensor(rank[:, 1:2], rank[:, 0:1], before_ps, ALU.add))
                ranks = narrow[:].bitcast(I16)
                halves = [slice(h * BANK, (h + 1) * BANK) for h in range(2)]

                def rank_ties(cols):
                    return mark(v.tensor_tensor_scan(ranks, ties[:, cols], ties[:, cols], rank[:, 1:2],
                                                     ALU.add, ALU.max))

                def keep_high_ties(cols):
                    return mark(v.scalar_tensor_tensor(ties[:, cols], ranks, CUT + 0.5, ties[:, cols],
                                                       ALU.is_gt, ALU.mult))

                def keep_larger(cols):
                    return mark(v.scalar_tensor_tensor(ties[:, cols], gate[:, cols], value, ties[:, cols],
                                                       ALU.is_gt, ALU.max))

                dve.wait_ge(rest_made, i(4, 4))
                if not (isinstance(pair, int) and pair + 1 >= pairs):
                    dve.wait_ge(hidden_made, i(1, 2))
                wait_for(rank_ties(halves[0]))
                v.tensor_copy(rank[:, 1:2], ranks[:, BANK - 1:BANK])
                wait_for(keep_high_ties(halves[0]))
                ranks_made = rank_ties(halves[1])
                larger = keep_larger(halves[0])
                wait_for(ranks_made)
                high_ties = keep_high_ties(halves[1])
                wait_for(larger)
                v.tensor_tensor(masked[:, halves[0]], masked[:, halves[0]], ties[:, halves[0]],
                                ALU.mult).then_inc(half_masked, 1)
                wait_for(high_ties)
                wait_for(keep_larger(halves[1]))
                v.tensor_tensor(masked[:, halves[1]], masked[:, halves[1]], ties[:, halves[1]],
                                ALU.mult).then_inc(masked_made, 1)
                assert done[0] == CHAIN, done
                for piece in range(2 * ADDS):
                    a, c = divmod(piece, ADDS)
                    dve.wait_ge(spread_made, i(2 * ADDS, piece + 1))
                    values = xs[:, 2 * s + a, :, c * BANK:(c + 1) * BANK]
                    gates = spread_ps[piece % SPREADS][:, 0:BANK].unsqueeze(1).to_broadcast([P, 2, BANK])
                    v.tensor_tensor(values, values, gates, ALU.add).then_inc(added, 1)

            each_pair(dve, body, body, body)


def kernel(x, L0_conv_W1, L0_conv_W2):
    import concourse.bacc as bacc
    from concourse.bass_utils import run_bass_kernel_spmd

    w1 = np.asarray(L0_conv_W1).reshape(HIDDEN, 2, QUARTERS, BANK).transpose(0, 2, 1, 3)
    w1 = w1.reshape(HIDDEN, QUARTERS, CHUNKS, CHUNK).transpose(3, 2, 1, 0)
    w1 = np.ascontiguousarray(w1.reshape(CHUNK, CHUNKS * QUARTERS, HIDDEN))
    w2 = np.asarray(L0_conv_W2).T.reshape(2, HALF_HIDDEN, PIXELS).transpose(1, 0, 2)
    table, count_table = constants()
    arrays = {"x": np.ascontiguousarray(x), "w1": w1, "w2": np.ascontiguousarray(w2),
              "table": table, "count_table": count_table}

    nc = bacc.Bacc("TRN2", target_bir_lowering=False, num_devices=1)
    ins = [nc.dram_tensor(k, a.shape, mybir.dt.from_np(a.dtype), kind="ExternalInput").ap() for k, a in arrays.items()]
    out = nc.dram_tensor("out", arrays["x"].shape, F32, kind="ExternalOutput").ap()
    gate_kernel(nc, *ins, out)
    result = run_bass_kernel_spmd(nc, [arrays], core_ids=[0])
    return result.results[0]["out"]
```
